# Optimizing a Trainium2 kernel written in Bass

```python
import numpy as np
import jax
import jax.numpy as jnp

def _softmax(x, axis=-1):
    return jax.nn.softmax(x, axis=axis)

def _gelu(x):
    return jax.nn.gelu(x, approximate=True)

def _silu(x):
    return jax.nn.silu(x)

def _sigmoid(x):
    return jax.nn.sigmoid(x)

def _layernorm(x, axis=-1, eps=1e-05):
    m = jnp.mean(x, axis=axis, keepdims=True)
    v = jnp.var(x, axis=axis, keepdims=True)
    return (x - m) / jnp.sqrt(v + eps)

def _scatter_add(tgt, idx, src, axis=0):
    return tgt.at[idx].add(src)

def _segment_sum(src, seg, n):
    return jax.ops.segment_sum(src, seg, n)
kernel_name = 'mk_seq_preln_d1_jaxref_r8_b0dca7'

def setup_inputs(seed: int=0):
    np.random.seed(seed)
    _w = jnp.asarray

    def _L0_attn_setup():
        import jax, jax.numpy as jnp
        import numpy as np
        B, S, D = (2, 256, 256)
        H, HD = (32, 128)
        P = H * HD
        K = 4
        F_ = 1024
        EPS = 1e-06

        def _rmsnorm(x, w, eps=EPS):
            xf = x.astype(jnp.float32)
            y = xf * jax.lax.rsqrt(jnp.mean(xf * xf, axis=-1, keepdims=True) + eps)
            return (y * w).astype(x.dtype)

        def _short_conv(x, w):
            k = w.shape[1]
            xp = jnp.pad(x, ((0, 0), (k - 1, 0), (0, 0)))
            y = sum((xp[:, j:j + x.shape[1], :] * w[:, j] for j in range(k)))
            return jax.nn.silu(y)

        def _l2norm(x, eps=1e-06):
            return x * jax.lax.rsqrt(jnp.sum(x * x, axis=-1, keepdims=True) + eps)

        def _kda(q, k, v, g, beta):
            scale = q.shape[-1] ** (-0.5)
            q = _l2norm(q) * scale
            k = _l2norm(k)
            tm = lambda a: jnp.swapaxes(a, 0, 1)
            qs, ks_, vs, gs, bs = (tm(q), tm(k), tm(v), tm(g), tm(beta))
            bsz, h, hd = (q.shape[0], q.shape[2], q.shape[3])
            S0 = jnp.zeros((bsz, h, hd, hd), jnp.float32)

            def step(St, inp):
                qt, kt, vt, gt, bt = inp
                St = St * jnp.exp(gt)[..., None]
                err = jnp.einsum('bhk,bhkv->bhv', kt, St)
                St = St + bt[..., None, None] * kt[..., None] * (vt - err)[..., None, :]
                ot = jnp.einsum('bhk,bhkv->bhv', qt, St)
                return (St, ot)
            _, o = jax.lax.scan(step, S0, (qs, ks_, vs, gs, bs))
            return jnp.swapaxes(o, 0, 1)
        key = jax.random.key(seed)
        ks = jax.random.split(key, 20)
        std = 0.02
        inp = {'x': jax.random.normal(ks[0], (B, S, D), jnp.float32), 'norm1_w': jnp.ones((D,), jnp.float32), 'wq': jax.random.normal(ks[1], (D, P), jnp.float32) * std, 'wk': jax.random.normal(ks[2], (D, P), jnp.float32) * std, 'wv': jax.random.normal(ks[3], (D, P), jnp.float32) * std, 'conv_q': jax.random.normal(ks[4], (P, K), jnp.float32) * 0.5, 'conv_k': jax.random.normal(ks[5], (P, K), jnp.float32) * 0.5, 'conv_v': jax.random.normal(ks[6], (P, K), jnp.float32) * 0.5, 'f_a': jax.random.normal(ks[7], (D, HD), jnp.float32) * std, 'f_b': jax.random.normal(ks[8], (HD, P), jnp.float32) * std, 'A_log': jnp.log(jax.random.uniform(ks[9], (H,), jnp.float32, 1.0, 16.0)), 'dt_bias': jnp.zeros((P,), jnp.float32), 'b_w': jax.random.normal(ks[10], (D, H), jnp.float32) * std, 'g_a': jax.random.normal(ks[11], (D, HD), jnp.float32) * std, 'g_b': jax.random.normal(ks[12], (HD, P), jnp.float32) * std, 'onorm_w': jnp.ones((HD,), jnp.float32), 'wo': jax.random.normal(ks[13], (P, D), jnp.float32) * std, 'norm2_w': jnp.ones((D,), jnp.float32), 'w1': jax.random.normal(ks[14], (D, F_), jnp.float32) * std, 'w2': jax.random.normal(ks[15], (F_, D), jnp.float32) * std, 'w3': jax.random.normal(ks[16], (D, F_), jnp.float32) * std}
        return inp
    _L0_attn_in = _L0_attn_setup()

    def _L0_ffn_setup():
        import jax, jax.numpy as jnp
        import numpy as np
        H, I, E, K = (256, 512, 8, 2)
        B, S = (1, 256)

        def _silu_mul(gu):
            d = gu.shape[-1] // 2
            return jax.nn.silu(gu[..., :d]) * gu[..., d:]
        key = jax.random.key(seed)
        ks = jax.random.split(key, 6)
        w_scale = 0.02
        return {'x': jax.random.normal(ks[0], (B, S, H), jnp.float32), 'gate_w': jax.random.normal(ks[1], (H, E), jnp.float32) * w_scale, 'base_gate_up': jax.random.normal(ks[2], (H, 2 * I), jnp.float32) * w_scale, 'base_down': jax.random.normal(ks[3], (I, H), jnp.float32) * w_scale, 'expert_gate_up': jax.random.normal(ks[4], (E, H, 2 * I), jnp.float32) * w_scale, 'expert_down': jax.random.normal(ks[5], (E, I, H), jnp.float32) * w_scale}
    _L0_ffn_in = _L0_ffn_setup()
    _d = {'L0_attn_x': _L0_attn_in['x'], 'L0_attn_norm1_w': _L0_attn_in['norm1_w'], 'L0_attn_wq': _L0_attn_in['wq'], 'L0_attn_wk': _L0_attn_in['wk'], 'L0_attn_wv': _L0_attn_in['wv'], 'L0_attn_conv_q': _L0_attn_in['conv_q'], 'L0_attn_conv_k': _L0_attn_in['conv_k'], 'L0_attn_conv_v': _L0_attn_in['conv_v'], 'L0_attn_f_a': _L0_attn_in['f_a'], 'L0_attn_f_b': _L0_attn_in['f_b'], 'L0_attn_A_log': _L0_attn_in['A_log'], 'L0_attn_dt_bias': _L0_attn_in['dt_bias'], 'L0_attn_b_w': _L0_attn_in['b_w'], 'L0_attn_g_a': _L0_attn_in['g_a'], 'L0_attn_g_b': _L0_attn_in['g_b'], 'L0_attn_onorm_w': _L0_attn_in['onorm_w'], 'L0_attn_wo': _L0_attn_in['wo'], 'L0_attn_norm2_w': _L0_attn_in['norm2_w'], 'L0_attn_w1': _L0_attn_in['w1'], 'L0_attn_w2': _L0_attn_in['w2'], 'L0_attn_w3': _L0_attn_in['w3'], 'L0_ffn_gate_w': _L0_ffn_in['gate_w'], 'L0_ffn_base_gate_up': _L0_ffn_in['base_gate_up'], 'L0_ffn_base_down': _L0_ffn_in['base_down'], 'L0_ffn_expert_gate_up': _L0_ffn_in['expert_gate_up'], 'L0_ffn_expert_down': _L0_ffn_in['expert_down']}
    _x0 = _d['L0_attn_x']
    _d['L0_attn_x'] = jax.random.normal(jax.random.fold_in(jax.random.key(seed), 1), (4, 512, 256), dtype=_x0.dtype)
    del _x0
    return _d

def reference(L0_attn_x, L0_attn_norm1_w, L0_attn_wq, L0_attn_wk, L0_attn_wv, L0_attn_conv_q, L0_attn_conv_k, L0_attn_conv_v, L0_attn_f_a, L0_attn_f_b, L0_attn_A_log, L0_attn_dt_bias, L0_attn_b_w, L0_attn_g_a, L0_attn_g_b, L0_attn_onorm_w, L0_attn_wo, L0_attn_norm2_w, L0_attn_w1, L0_attn_w2, L0_attn_w3, L0_ffn_gate_w, L0_ffn_base_gate_up, L0_ffn_base_down, L0_ffn_expert_gate_up, L0_ffn_expert_down):

    def _L0_attn_ref(x, norm1_w, wq, wk, wv, conv_q, conv_k, conv_v, f_a, f_b, A_log, dt_bias, b_w, g_a, g_b, onorm_w, wo, norm2_w, w1, w2, w3):
        import jax, jax.numpy as jnp
        import numpy as np
        B, S, D = (2, 256, 256)
        H, HD = (32, 128)
        P = H * HD
        K = 4
        F_ = 1024
        EPS = 1e-06

        def _rmsnorm(x, w, eps=EPS):
            xf = x.astype(jnp.float32)
            y = xf * jax.lax.rsqrt(jnp.mean(xf * xf, axis=-1, keepdims=True) + eps)
            return (y * w).astype(x.dtype)

        def _short_conv(x, w):
            k = w.shape[1]
            xp = jnp.pad(x, ((0, 0), (k - 1, 0), (0, 0)))
            y = sum((xp[:, j:j + x.shape[1], :] * w[:, j] for j in range(k)))
            return jax.nn.silu(y)

        def _l2norm(x, eps=1e-06):
            return x * jax.lax.rsqrt(jnp.sum(x * x, axis=-1, keepdims=True) + eps)

        def _kda(q, k, v, g, beta):
            scale = q.shape[-1] ** (-0.5)
            q = _l2norm(q) * scale
            k = _l2norm(k)
            tm = lambda a: jnp.swapaxes(a, 0, 1)
            qs, ks_, vs, gs, bs = (tm(q), tm(k), tm(v), tm(g), tm(beta))
            bsz, h, hd = (q.shape[0], q.shape[2], q.shape[3])
            S0 = jnp.zeros((bsz, h, hd, hd), jnp.float32)

            def step(St, inp):
                qt, kt, vt, gt, bt = inp
                St = St * jnp.exp(gt)[..., None]
                err = jnp.einsum('bhk,bhkv->bhv', kt, St)
                St = St + bt[..., None, None] * kt[..., None] * (vt - err)[..., None, :]
                ot = jnp.einsum('bhk,bhkv->bhv', qt, St)
                return (St, ot)
            _, o = jax.lax.scan(step, S0, (qs, ks_, vs, gs, bs))
            return jnp.swapaxes(o, 0, 1)
        bsz, seq, _ = x.shape
        h = _rmsnorm(x, norm1_w)
        q = _short_conv(h @ wq, conv_q).reshape(bsz, seq, H, HD)
        k = _short_conv(h @ wk, conv_k).reshape(bsz, seq, H, HD)
        v = _short_conv(h @ wv, conv_v).reshape(bsz, seq, H, HD)
        g = (h @ f_a @ f_b).reshape(bsz, seq, H, HD).astype(jnp.float32)
        g = g + dt_bias.reshape(H, HD)
        g = -jnp.exp(A_log)[:, None] * jax.nn.softplus(g)
        beta = jax.nn.sigmoid((h @ b_w).astype(jnp.float32))
        o = _kda(q.astype(jnp.float32), k.astype(jnp.float32), v.astype(jnp.float32), g, beta)
        gate = (h @ g_a @ g_b).reshape(bsz, seq, H, HD)
        og = o * jax.nn.sigmoid(gate.astype(jnp.float32))
        og = og * jax.lax.rsqrt(jnp.mean(og * og, axis=-1, keepdims=True) + EPS)
        o = (og * onorm_w).astype(x.dtype).reshape(bsz, seq, P)
        x = x + o @ wo
        h2 = _rmsnorm(x, norm2_w)
        ffn = jax.nn.silu(h2 @ w1) * (h2 @ w3) @ w2
        return x + ffn

    def _L0_ffn_ref(x, gate_w, base_gate_up, base_down, expert_gate_up, expert_down):
        import jax, jax.numpy as jnp
        import numpy as np
        H, I, E, K = (256, 512, 8, 2)
        B, S = (1, 256)

        def _silu_mul(gu):
            d = gu.shape[-1] // 2
            return jax.nn.silu(gu[..., :d]) * gu[..., d:]
        base_y = _silu_mul(x @ base_gate_up) @ base_down
        b, s, h = x.shape
        xf = x.reshape(-1, h)
        n = xf.shape[0]
        n_exp = gate_w.shape[1]
        probs = jax.nn.softmax((xf @ gate_w).astype(jnp.float32), axis=-1)
        w, idx = jax.lax.top_k(probs, K)
        w = (w / w.sum(axis=-1, keepdims=True)).astype(x.dtype)
        comb = jnp.zeros((n, n_exp), x.dtype).at[jnp.arange(n)[:, None], idx].add(w)
        out = jnp.zeros_like(xf)
        for e in range(n_exp):
            y = _silu_mul(xf @ expert_gate_up[e]) @ expert_down[e]
            out = out + comb[:, e:e + 1] * y
        return out.reshape(b, s, h) + base_y
    x = L0_attn_x
    x = x + _L0_attn_ref(_layernorm(x, axis=-1), L0_attn_norm1_w, L0_attn_wq, L0_attn_wk, L0_attn_wv, L0_attn_conv_q, L0_attn_conv_k, L0_attn_conv_v, L0_attn_f_a, L0_attn_f_b, L0_attn_A_log, L0_attn_dt_bias, L0_attn_b_w, L0_attn_g_a, L0_attn_g_b, L0_attn_onorm_w, L0_attn_wo, L0_attn_norm2_w, L0_attn_w1, L0_attn_w2, L0_attn_w3)
    x = x + _L0_ffn_ref(_layernorm(x, axis=-1), L0_ffn_gate_w, L0_ffn_base_gate_up, L0_ffn_base_down, L0_ffn_expert_gate_up, L0_ffn_expert_down)
    return x

_drawn_inputs = setup_inputs


def setup_inputs(seed=0):
    import zlib

    import numpy as np

    out = dict(_drawn_inputs(seed))
    spreads = {'L0_attn_norm1_w': (1.0, 0.2),
     'L0_attn_dt_bias': (0.0, 0.8),
     'L0_attn_onorm_w': (1.0, 0.2),
     'L0_attn_norm2_w': (1.0, 0.6)}
    factors = {'L0_attn_f_a': 8.0,
     'L0_attn_f_b': 8.0,
     'L0_attn_g_a': 7.375,
     'L0_attn_g_b': 7.372,
     'L0_attn_w1': 3.004,
     'L0_attn_w2': 2.968,
     'L0_attn_w3': 2.974,
     'L0_ffn_gate_w': 7.862,
     'L0_ffn_base_gate_up': 4.822,
     'L0_ffn_base_down': 4.82,
     'L0_ffn_expert_gate_up': 6.784,
     'L0_ffn_expert_down': 6.783}
    for name, (base, spread) in spreads.items():
        noise = np.random.default_rng([zlib.crc32(name.encode()), seed]).standard_normal(out[name].shape)
        drawn = base * np.exp(spread * noise) if base else spread * noise
        out[name] = jnp.asarray(drawn.astype(out[name].dtype))
    for name, factor in factors.items():
        out[name] = (out[name] * factor).astype(out[name].dtype)
    return out
```

```python
from contextlib import ExitStack

import numpy as np
import concourse.bass as bass
from concourse import mybir

F32 = mybir.dt.float32
U32 = mybir.dt.uint32
ALU = mybir.AluOpType
ACT = mybir.ActivationFunctionType
AX = mybir.AxisListType

B, S, D = 4, 512, 256
H, HD = 32, 128
TAPS = 4
TOK = B * S
NT = TOK // 128
DC = D // 128
TPB = S // 128
UNITS = B * H
C = 64
NCH = S // C
SUB = 16
NSUB = S // SUB
F = 1024
E = 8
I = 512
LN_EPS, RMS_EPS, L2_EPS = 1e-5, 1e-6, 1e-6
SP_MAX = 40.0
TINY = 2.0 ** -40
LEVELS = [1, 2, 4, 8, 16, 32]


def shape_constants():
    j = np.arange(128)[:, None] % 32
    i = np.arange(32)[None, :]
    lev = []
    for m in LEVELS[:5]:
        lev.append((j // (2 * m) == i // (2 * m)) & (j % (2 * m) < m) & (i % (2 * m) >= m))
    both = [np.concatenate([x, x], 1) for x in lev]
    masks = np.concatenate([*both[1:], (j == i)], 1).astype(np.float32)
    first = both[0].astype(np.float32)
    r, c = np.arange(128)[:, None], np.arange(128)[None, :]
    up16 = ((r // 32 == c // 32) & (r % 32 >= 16) & (c % 32 < 16)).astype(np.float32)
    blk = np.zeros((128, 8, SUB), np.float32)
    blk[np.arange(128), np.arange(128) // SUB, :] = 1
    return {
        "c_masks": masks, "c_first": first, "c_up16": up16, "c_blk": blk.reshape(128, 128),
        "c_ident": np.eye(128, dtype=np.float32),
        "c_eye": np.tile(np.eye(SUB, dtype=np.float32).reshape(1, SUB * SUB), (NSUB, 1)),
    }


def at(eng, sem, unit, per, k):
    if isinstance(unit, int) and unit < 0:
        return
    eng.wait_ge(sem, unit * per + k)


def bc(ap, n):
    return ap.unsqueeze(2).to_broadcast([ap.shape[0], ap.shape[1], n])


def tiles_bc(ap, n):
    return ap.unsqueeze(1).to_broadcast([ap.shape[0], n, ap.shape[1]])


def build(nc, t, out):
    with ExitStack() as whole:
        def keep(name, shape, dt=F32):
            return whole.enter_context(nc.sbuf_tensor(name, shape, dt))

        ident = keep("ident", [128, 128])
        acc = keep("acc", [128, NT, D])
        banks = [whole.enter_context(nc.psum_tensor(f"bank{i}", [128, 512], F32)) for i in range(8)]
        with ExitStack() as ctx:
            hT = ctx.enter_context(nc.sbuf_tensor("hT", [128, DC, TOK], F32))
            fT = ctx.enter_context(nc.sbuf_tensor("fT", [128, TOK], F32))
            gT = ctx.enter_context(nc.sbuf_tensor("gT", [128, TOK], F32))
            beta = ctx.enter_context(nc.sbuf_tensor("beta", [128, H, NT], F32))
            pre_norm(nc, t, ident, acc, banks, hT, fT, gT, beta)
            attention(nc, t, ident, acc, banks, hT, fT, gT, beta)
        feed_forward(nc, t, ident, acc, banks, out)


def pre_norm(nc, t, ident, acc, banks, hT, fT, gT, beta):
    with ExitStack() as ctx:
        def sb(name, shape, dt=F32):
            return ctx.enter_context(nc.sbuf_tensor(name, shape, dt))

        def sem(name):
            return ctx.enter_context(nc.semaphore(name))

        x = sb("x", [128, NT, D])
        stats = sb("stats", [128, NT, 6])
        mv = sb("mv", [128, NT, 2])
        r1 = sb("r1", [128, 6, NT])
        hrow = sb("hrow", [128, 4, D])
        w1n = sb("w1n", [128, DC])
        fa = sb("fa", [128, DC, HD])
        ga = sb("ga", [128, DC, HD])
        bw = sb("bw", [128, DC, H])

        x_loaded, w_loaded = sem("x_loaded"), sem("w_loaded")
        stat_step, norm_step, rows_ready = sem("stat_step"), sem("norm_step"), sem("rows_ready")
        root_ready, hT_ready = sem("root_ready"), sem("hT_ready")
        tr_done, low_done, beta_done = sem("tr_done"), sem("low_done"), sem("beta_done")
        f_ready, g_ready, beta_ready = sem("f_ready"), sem("g_ready"), sem("beta_ready")
        block = ctx.enter_context(nc.Block())
        xv = t["L0_attn_x"].rearrange("b (n p) d -> p (b n) d", p=128)

        @block.sync
        def _(sp):
            for i in range(4):
                sp.dma_start(x[:, 4 * i:4 * i + 4, :], xv[:, 4 * i:4 * i + 4, :]).then_inc(x_loaded, 16)
                sp.wait_ge(x_loaded, 16 * i + 16)
            sp.dma_start(ident[:, :], t["c_ident"]).then_inc(w_loaded, 16)
            sp.dma_start(w1n[:, :], t["L0_attn_norm1_w"].rearrange("(c p) -> p c", p=128), allow_slow_non_contiguous=True).then_inc(w_loaded, 16)
            sp.dma_start(fa[:, :, :], t["L0_attn_f_a"].rearrange("(c p) m -> p c m", p=128)).then_inc(w_loaded, 16)
            sp.dma_start(ga[:, :, :], t["L0_attn_g_a"].rearrange("(c p) m -> p c m", p=128)).then_inc(w_loaded, 16)
            sp.dma_start(bw[:, :, :], t["L0_attn_b_w"].rearrange("(c p) m -> p c m", p=128)).then_inc(w_loaded, 16)

        @block.vector
        def _(dve):
            for i in range(NT):
                dve.wait_ge(x_loaded, 16 * (i // 4 + 1))
                dve.bn_stats(stats[:, i, :], x[:, i, :]).then_inc(stat_step, 1)
            for i in range(NT):
                dve.wait_ge(stat_step, i + 1)
                dve.bn_aggr(mv[:, i, :], stats[:, i, :]).then_inc(norm_step, 1)
            dve.wait_ge(norm_step, NT)
            dve.tensor_scalar(r1[:, 0, :], mv[:, :, 1], LN_EPS, None, ALU.add).then_inc(norm_step, 1)
            dve.wait_ge(root_ready, 1)
            dve.reciprocal(r1[:, 2, :], r1[:, 1, :]).then_inc(norm_step, 1)
            dve.wait_ge(norm_step, NT + 2)
            dve.tensor_tensor(r1[:, 3, :], r1[:, 2, :], r1[:, 2, :], ALU.mult).then_inc(norm_step, 1)
            dve.wait_ge(norm_step, NT + 3)
            dve.tensor_tensor(r1[:, 4, :], r1[:, 3, :], mv[:, :, 1], ALU.mult).then_inc(norm_step, 1)
            dve.wait_ge(norm_step, NT + 4)
            dve.tensor_scalar(r1[:, 3, :], r1[:, 4, :], RMS_EPS, None, ALU.add).then_inc(norm_step, 1)
            dve.wait_ge(root_ready, 2)
            dve.reciprocal(r1[:, 5, :], r1[:, 4, :]).then_inc(norm_step, 1)
            dve.wait_ge(norm_step, NT + 6)
            for i in range(NT):
                dve.tensor_scalar(acc[:, i, :], x[:, i, :], mv[:, i, 0:1], r1[:, 2, i:i + 1],
                                  ALU.subtract, ALU.mult).then_inc(norm_step, 1)
                dve.wait_ge(norm_step, NT + 7 + i)
                if i >= 4:
                    dve.wait_ge(tr_done, 2 * (i // 4))
                dve.tensor_scalar(hrow[:, i % 4, :], acc[:, i, :], r1[:, 5, i:i + 1], None,
                                  ALU.mult).then_inc(rows_ready, 1)
            for i in range(4):
                dve.wait_ge(low_done, 2 * i + 2)
                dve.tensor_copy(gT[:, 512 * i:512 * i + 512], banks[2 + 2 * (i % 2) + 1][:, :]).then_inc(g_ready, 1)

        @block.scalar
        def _(act):
            act.wait_ge(norm_step, NT + 1)
            act.activation(r1[:, 1, :], r1[:, 0, :], ACT.Sqrt).then_inc(root_ready, 1)
            act.wait_ge(norm_step, NT + 5)
            act.activation(r1[:, 4, :], r1[:, 3, :], ACT.Sqrt).then_inc(root_ready, 1)
            act.wait_ge(w_loaded, 80)
            for i in range(4):
                for c in range(DC):
                    act.wait_ge(tr_done, 2 * i + c + 1)
                    act.activation(hT[:, c, 512 * i:512 * i + 512], banks[c][:, :], ACT.Copy,
                                   scale=w1n[:, c:c + 1]).then_inc(hT_ready, 1)
            for i in range(4):
                act.wait_ge(low_done, 2 * i + 1)
                act.activation(fT[:, 512 * i:512 * i + 512], banks[2 + 2 * (i % 2)][:, :], ACT.Copy).then_inc(f_ready, 1)
            act.wait_ge(beta_done, 1)
            act.activation(beta[:, :, :].rearrange("p h n -> p n h"),
                           banks[6][:, :].rearrange("p (n h) -> p n h", h=H), ACT.Sigmoid).then_inc(beta_ready, 1)
            act.wait_ge(beta_ready, 1)

        @block.tensor
        def _(pe):
            pe.wait_ge(w_loaded, 80)
            for i in range(4):
                pe.wait_ge(rows_ready, 4 * i + 4)
                for c in range(DC):
                    if i:
                        pe.wait_ge(hT_ready, 2 * (i - 1) + c + 1)
                    for n in range(4):
                        mm = pe.transpose(banks[c][:, 128 * n:128 * n + 128], hrow[:, n, 128 * c:128 * c + 128], ident[:, :])
                    mm.then_inc(tr_done, 1)
            pe.wait_ge(hT_ready, 8)
            for i in range(4):
                for k, w in enumerate((fa, ga)):
                    if i >= 2:
                        pe.wait_ge((f_ready, g_ready)[k], i - 1)
                    for c in range(DC):
                        mm = pe.matmul(banks[2 + 2 * (i % 2) + k][:, :], w[:, c, :], hT[:, c, 512 * i:512 * i + 512],
                                       start=(c == 0), stop=(c == DC - 1))
                    mm.then_inc(low_done, 1)
            for n in range(NT):
                for c in range(DC):
                    mm = pe.matmul(banks[6][:, H * n:H * n + H], hT[:, c, 128 * n:128 * n + 128], bw[:, c, :],
                                   start=(c == 0), stop=(c == DC - 1))
            mm.then_inc(beta_done, 1)


def attention(nc, t, ident, acc, banks, hT, fT, gT, beta):
    with ExitStack() as ctx:
        def sb(name, shape, dt=F32):
            return ctx.enter_context(nc.sbuf_tensor(name, shape, dt))

        def sem(name):
            return ctx.enter_context(nc.semaphore(name))

        masks = sb("masks", [128, 4 * 64 + 32])
        first = sb("first", [128, 64])
        up16 = sb("up16", [128, 128])
        blk = sb("blk", [128, 128])
        eye = sb("eye", [NSUB, SUB * SUB])
        ones = sb("ones", [128, 1])
        onorm = sb("onorm", [128, 1])
        NPAR = 3 * TAPS + 2
        par_all = sb("par_all", [128, H, NPAR])
        par_one = sb("par_one", [128, NPAR])
        alog = sb("alog", [128, H])
        w_in = [sb(f"w_{x}", [128, DC, HD]) for x in "kqv"]
        fb, gb = sb("fb", [128, HD]), sb("gb", [128, HD])
        wo = sb("wo", [128, D])
        par = sb("par", [128, 2, NPAR])
        xp = [sb(f"xp_{x}", [128, S + TAPS - 1]) for x in "kqv"]
        y = [sb(f"y_{x}", [128, S]) for x in "kqv"]
        sg = [sb(f"sg_{x}", [128, S]) for x in "kqv"]
        gx, ge = sb("gx", [128, S]), sb("ge", [128, S])
        sq = sb("sq", [128, 2, S])
        kr = sb("kr", [128, B, S])
        kq = sb("kq", [128, B, 3, S])
        vt = sb("vt", [128, B, S])
        dec = sb("dec", [128, B, S])
        tot = sb("tot", [128, B, S])
        gate = sb("gate", [128, B, TPB, HD])
        ab = sb("ab", [128, B, TPB, 2, 128])
        r2 = sb("r2", [128, B, 2, TPB])
        bp = sb("bp", [128, B, 3, TPB])
        rk = sb("rk", [128, B, 2, TPB])
        comp = sb("comp", [128, TPB, 64])
        zm = sb("zm", [128, TPB, 128])
        own = sb("own", [128, TPB, 32])
        lb, bb = sb("lb", [NSUB, SUB, SUB]), sb("bb", [NSUB, SUB])
        xs, pr = sb("xs", [NSUB, SUB, SUB]), sb("pr", [NSUB, SUB, SUB])
        xc = sb("xc", [128, TPB, SUB])
        X, XT, Y = (sb(n, [128, TPB, 128]) for n in ("X", "XT", "Y"))
        vs, ks = sb("vs", [128, TPB, HD]), sb("ks", [128, TPB, HD])
        kh = sb("kh", [128, 2, TPB, HD])
        tv = sb("tv", [128, 2, TPB, HD])
        tk = sb("tk", [128, 2, TPB, 128])
        U = sb("U", [128, 2, HD])
        St = sb("St", [128, 2, HD])
        og = sb("og", [128, TPB, HD])
        ogs = sb("ogs", [128, HD])
        oss = sb("oss", [128, TPB])
        fin = sb("fin", [128, 5, TPB])
        ogT = sb("ogT", [128, TPB, 128])
        a_dram = nc.dram_tensor("a_dram", (2, 128, TPB, 32), F32).ap()
        b_dram = nc.dram_tensor("b_dram", (2, 128, TPB), F32).ap()
        x_dram = nc.dram_tensor("x_dram", (2, NSUB, SUB * SUB), F32).ap()

        PJ, SC, MI = banks[0:2], banks[2:4], banks[4:6]
        CH, OB = banks[6], banks[7]
        SUMS = SC[1][:, 384:384 + 2 * TPB]

        const_loaded, const_ready, nega_exp = sem("const_loaded"), sem("const_ready"), sem("nega_exp")
        w_loaded = [sem(f"w_loaded_{x}") for x in ("k", "q", "v", "f", "g")]
        wo_loaded = sem("wo_loaded")
        proj_done, lev_done, sums_done = sem("proj_done"), sem("lev_done"), sem("sums_done")
        vtr_done, ktr_done, khtr_done = sem("vtr_done"), sem("ktr_done"), sem("khtr_done")
        xt_done, y_done, z_done = sem("xt_done"), sem("y_done"), sem("z_done")
        tv_done, tk_done, ogtr_done, wo_done = sem("tv_done"), sem("tk_done"), sem("ogtr_done"), sem("wo_done")
        ups_done, sps_done, o_done = sem("ups_done"), sem("sps_done"), sem("o_done")
        conv_step, gmin_ready, sp_ready = sem("conv_step"), sem("gmin_ready"), sem("sp_ready")
        norm_step, bv_ready = sem("knorm_step"), sem("bv_ready")
        scale_step, lev_read = sem("scale_step"), sem("lev_read")
        vs_ready, ks_ready, y_ready = sem("vs_ready"), sem("ks_ready"), sem("y_ready")
        x_merged, xt_merged = sem("x_merged"), sem("xt_merged")
        u_ready, s_ready = sem("u_ready"), sem("s_ready")
        og_ready, fin_step, acc_step = sem("og_ready"), sem("fin_step"), sem("acc_step")
        proj_read, sig_ready, g_step, dec_ready = sem("proj_read"), sem("sig_ready"), sem("g_step"), sem("dec_ready")
        sq_ready, rk_step, ab_ready, xt_ready = sem("sq_ready"), sem("rk_step"), sem("ab_ready"), sem("xt_ready")
        kh_ready, tv_ready, tk_ready = sem("kh_ready"), sem("tv_ready"), sem("tk_ready")
        oss_ready, fin_ready, ogt_ready = sem("oss_ready"), sem("fin_ready"), sem("ogt_ready")
        tap_ready = sem("tap_ready")
        par_ready, qkv_ready, sub_step, x_ready = sem("par_ready"), sem("qkv_ready"), sem("sub_step"), sem("x_ready")
        ab_out, ab_in, x_out, x_in = sem("ab_out"), sem("ab_in"), sem("x_out"), sem("x_in")
        SUBS = 2 + 2 * (SUB - 1)
        ROUNDED = (1, 3, 5)

        def after_scale(k):
            return 2 + 3 * k + 2 * sum(r < k for r in ROUNDED)

        SCALES = after_scale(len(LEVELS))

        def slots(slot):
            for n in range(-4, 4):
                slot(0, n)
            yield
            for b in range(5):
                slot(H - 1, b)

        def unit(h, b, d):
            hh, bb_ = h + (b + d) // B, (b + d) % B
            u = hh * B + bb_
            return hh, bb_, u, (not isinstance(u, int)) or 0 <= u < UNITS

        def run(eng, slot):
            steps = slots(slot)
            next(steps)
            with eng.Fori(1, H - 1) as h:
                for b in range(B):
                    slot(h, b)
            next(steps, None)

        block = ctx.enter_context(nc.Block())

        @block.sync
        def _(sp):
            def load(dst, src, **how):
                sp.dma_start(dst, src, **how).then_inc(const_loaded, 16)

            load(masks[:, :], t["c_masks"])
            load(first[:, :], t["c_first"])
            load(up16[:, :], t["c_up16"])
            load(blk[:, :], t["c_blk"])
            load(eye[:, :], t["c_eye"])
            load(onorm[:, :], t["L0_attn_onorm_w"].rearrange("(p a) -> p a", a=1))
            for i, x in enumerate("kqv"):
                load(par_all[:, :, TAPS * i:TAPS * i + TAPS], t[f"L0_attn_conv_{x}"].rearrange("(h p) k -> p h k", p=128))
            load(par_all[:, :, 12], t["L0_attn_dt_bias"].rearrange("(h p) -> p h", p=128), allow_slow_non_contiguous=True)
            load(alog[:, :], t["L0_attn_A_log"].rearrange("(a h) -> a h", a=1).to_broadcast([128, H]))

            w_dst = [*(w[:, :, :] for w in w_in), fb[:, :], gb[:, :]]
            w_src = [*(t[f"L0_attn_w{x}"].rearrange("(c p) (h m) -> h p c m", p=128, m=HD) for x in "kqv"),
                     t["L0_attn_f_b"].rearrange("p (h m) -> h p m", m=HD),
                     t["L0_attn_g_b"].rearrange("p (h m) -> h p m", m=HD)]
            wo_src = t["L0_attn_wo"].rearrange("(h p) n -> h p n", p=128)
            for i in range(5):
                sp.dma_start(w_dst[i], w_src[i][0]).then_inc(w_loaded[i], 16)
            sp.dma_start(wo[:, :], wo_src[0]).then_inc(wo_loaded, 16)

            def more_heads(hh):
                return not (isinstance(hh, int) and hh >= H - 1)

            def weights(h, b, some):
                hh, bh, u, live = unit(h, b, 3)
                if live and bh == B - 1 and more_heads(hh):
                    for i in some:
                        at(sp, proj_done, u, 5, i + 1)
                        sp.dma_start(w_dst[i], w_src[i][hh + 1]).then_inc(w_loaded[i], 16)

            def slot(h, b):
                _, bh, u, live = unit(h, b, 1)
                p = bh % 2
                if live:
                    at(sp, sub_step, u, SUBS, SUBS)
                    sp.dma_start(x_dram[p], xs[:, :, :].rearrange("p i j -> p (i j)")).then_inc(x_out, 16)
                    at(sp, x_out, u, 16, 16)
                    at(sp, x_ready, u - 1, 1, 1)
                    sp.dma_start(xc[:, :, :], x_dram[p].rearrange("(n c) (i j) -> (c i) n j", n=TPB, j=SUB)).then_inc(x_in, 16)
                weights(h, b, (0, 1, 2, 3))
                _, bh, u, live = unit(h, b, 2)
                p = bh % 2
                if live:
                    at(sp, lev_read, u, 10, 8)
                    sp.dma_start(a_dram[p], comp[:, :, 0:32]).then_inc(ab_out, 16)
                    at(sp, norm_step, u, 5, 4)
                    sp.dma_start(b_dram[p], bp[:, bh, 0, :]).then_inc(ab_out, 16)
                    at(sp, ab_out, u, 32, 32)
                    at(sp, sub_step, u - 1, SUBS, SUBS)
                    av = a_dram[p].rearrange("(g s j) n (z i) -> n g s j z i", s=2, j=SUB, z=2)
                    for n in range(TPB):
                        for s in range(2):
                            sp.dma_start(lb[8 * n + s:8 * n + 8:2, :, :], av[n, :, s, :, s, :]).then_inc(ab_in, 16)
                    for n in range(TPB):
                        sp.dma_start(bb[8 * n:8 * n + 8, :], b_dram[p].rearrange("(c i) n -> n c i", i=SUB)[n],
                                     allow_slow_non_contiguous=True).then_inc(ab_in, 16)
                weights(h, b, (4,))
                hh, bh, u, live = unit(h, b, -1)
                if live and bh == B - 1 and more_heads(hh):
                    at(sp, wo_done, u, 2, 2)
                    sp.dma_start(wo[:, :], wo_src[hh + 1]).then_inc(wo_loaded, 16)

            run(sp, slot)

        @block.gpsimd
        def _(pool):
            pool.memset(ones[:, :], 1.0).then_inc(const_ready, 1)
            pool.memset(par_one[:, :], 1.0).then_inc(const_ready, 1)
            for i in range(3):
                pool.memset(xp[i][:, 0:TAPS - 1], 0.0).then_inc(const_ready, 1)
            pool.memset(ab[:, :, :, :, :], 0.0).then_inc(const_ready, 1)
            pool.memset(U[:, :, :], 0.0).then_inc(const_ready, 1)
            pool.wait_ge(const_loaded, 16 * 11)

            def substitute(h, b):
                _, bh, u, live = unit(h, b, 1)
                if not live:
                    return
                at(pool, ab_in, u, 16 * 12, 16 * 12)
                pool.tensor_tensor(lb[:, :, :], lb[:, :, :], tiles_bc(bb[:, :], SUB), ALU.mult).then_inc(sub_step, 1)
                at(pool, x_out, u - 1, 16, 16)
                pool.tensor_tensor(xs[:, :, :].rearrange("p i j -> p (i j)"), eye[:, :], eye[:, :], ALU.mult).then_inc(sub_step, 1)
                for j in range(SUB - 1):
                    n = SUB - 1 - j
                    at(pool, sub_step, u, SUBS, 2 + 2 * j)
                    pool.tensor_tensor(pr[:, 0:n, 0:j + 1], bc(lb[:, j, j + 1:SUB], j + 1),
                                       tiles_bc(xs[:, j, 0:j + 1], n), ALU.mult).then_inc(sub_step, 1)
                    at(pool, sub_step, u, SUBS, 3 + 2 * j)
                    pool.tensor_tensor(xs[:, j + 1:SUB, 0:j + 1], xs[:, j + 1:SUB, 0:j + 1], pr[:, 0:n, 0:j + 1],
                                       ALU.subtract).then_inc(sub_step, 1)

            def expand(h, b):
                _, bh, u, live = unit(h, b, 1)
                if not live:
                    return
                at(pool, x_in, u, 16, 16)
                at(pool, y_done, u - 1, 2, 2)
                pool.tensor_tensor(X[:, :, :].rearrange("p n (c j) -> p n c j", j=SUB),
                                   xc[:, :, :].unsqueeze(2).to_broadcast([128, TPB, 8, SUB]),
                                   blk[:, :].rearrange("p (c j) -> p c j", j=SUB).unsqueeze(1).to_broadcast([128, TPB, 8, SUB]),
                                   ALU.mult).then_inc(x_ready, 1)

            def multiply(h, b, i):
                _, bh, u, live = unit(h, b, 3)
                if not live:
                    return
                at(pool, sig_ready, u, 3, i + 1)
                if i == 0:
                    at(pool, khtr_done, u - 4, 1, 1)
                if i == 1:
                    at(pool, o_done, u - 4, 8, 8)
                if i == 2:
                    at(pool, vtr_done, u - 4, 1, 1)
                dst = (kr[:, bh, :], kq[:, bh, 2, :], vt[:, bh, :])[i]
                pool.tensor_tensor(dst, y[i][:, :], sg[i][:, :], ALU.mult).then_inc(qkv_ready, 1)

            def slot(h, b):
                substitute(h, b)
                expand(h, b)
                multiply(h, b, 0)
                multiply(h, b, 1)
                multiply(h, b, 2)

            run(pool, slot)


        @block.tensor
        def _(pe):
            pe.wait_ge(const_ready, 8)
            pe.wait_ge(const_loaded, 16 * 11)

            def project(h, b, i):
                hh, bh, u, live = unit(h, b, 3)
                if not live:
                    return
                bank = PJ[(bh + i) % 2]
                at(pe, w_loaded[i], hh, 16, 16)
                if i >= 2:
                    at(pe, proj_read, u, 5, i - 1)
                else:
                    at(pe, proj_read, u - 1, 5, i + 4)
                tok = slice(S * bh, S * bh + S)
                if i == 3:
                    mm = pe.matmul(bank[:, :], fb[:, :], fT[:, tok], start=True, stop=True)
                elif i < 3:
                    for c in range(DC):
                        mm = pe.matmul(bank[:, :], w_in[i][:, c, :], hT[:, c, tok], start=(c == 0), stop=(c == DC - 1))
                else:
                    for n in range(TPB):
                        mm = pe.matmul(bank[:, 128 * n:128 * n + 128], gT[:, S * bh + 128 * n:S * bh + 128 * n + 128],
                                       gb[:, :], start=True, stop=True)
                mm.then_inc(proj_done, 1)

            def sums(h, b):
                _, bh, u, live = unit(h, b, 2)
                if not live:
                    return
                at(pe, sq_ready, u, 2, 2)
                at(pe, lev_read, u, 10, 6)
                for i in range(2):
                    for n in range(TPB):
                        mm = pe.matmul(SUMS[:, TPB * i + n:TPB * i + n + 1], sq[:, i, 128 * n:128 * n + 128],
                                       ones[:, :], start=True, stop=True)
                mm.then_inc(sums_done, 1)

            def level(h, b, k):
                _, bh, u, live = unit(h, b, 2)
                if not live:
                    return
                at(pe, scale_step, u, SCALES, after_scale(k))
                if k >= 2:
                    at(pe, lev_read, u, 10, k + 1)
                else:
                    at(pe, lev_read, u - 1, 10, 7 + 3 * k)
                    if k:
                        at(pe, norm_step, u - 1, 5, 2)
                bank = SC[k % 2]
                if k < 5:
                    w = 3 if k == 0 else 2
                    for n in range(TPB):
                        for g in range(4):
                            lo = 128 * n + 32 * g
                            mm = pe.matmul(bank[32 * g:32 * g + 32, 32 * w * n:32 * w * n + 32 * w],
                                           kr[:, bh, lo:lo + 32], kq[:, bh, 0:w, lo:lo + 32], start=True, stop=True)
                else:
                    for n in range(TPB):
                        for g in (0, 64):
                            lo = 128 * n + g
                            mm = pe.matmul(bank[g:g + 32, 64 * n:64 * n + 64],
                                           kr[:, bh, lo:lo + 32], kq[:, bh, 0:2, lo + 32:lo + 64], start=True, stop=True)
                mm.then_inc(lev_done, 1)

            def transpose4(bank, src):
                for n in range(TPB):
                    mm = pe.transpose(bank[:, 128 * n:128 * n + 128], src(n), ident[:, :])
                return mm

            def product4(bank, lhsT, rhs):
                for n in range(TPB):
                    mm = pe.matmul(bank[:, 128 * n:128 * n + 128], lhsT(n), rhs(n), start=True, stop=True)
                return mm

            def inverse(h, b, part):
                _, bh, u, live = unit(h, b, 1)
                if not live:
                    return
                tok = lambda n: slice(128 * n, 128 * n + 128)
                if part == "V":
                    at(pe, qkv_ready, u, 3, 3)
                    at(pe, tk_ready, u - 1, 1, 1)
                    transpose4(MI[1], lambda n: vt[:, bh, tok(n)]).then_inc(vtr_done, 1)
                elif part == "K":
                    at(pe, scale_step, u, SCALES, SCALES)
                    at(pe, vs_ready, u, 4, 4)
                    transpose4(MI[1], lambda n: kq[:, bh, 0, tok(n)]).then_inc(ktr_done, 1)
                elif part == "KH":
                    at(pe, ks_ready, u, 4, 4)
                    transpose4(MI[1], lambda n: kr[:, bh, tok(n)]).then_inc(khtr_done, 1)
                elif part == "XT":
                    at(pe, x_ready, u, 1, 1)
                    at(pe, acc_step, u - 2, 4, 4)
                    transpose4(MI[0], lambda n: X[:, n, :]).then_inc(xt_done, 1)
                elif part == "Y":
                    at(pe, kh_ready, u, 1, 1)
                    at(pe, lev_read, u, 10, 10)
                    at(pe, ab_ready, u, 4, 4)
                    product4(MI[1], lambda n: ab[:, bh, n, 0, :], lambda n: X[:, n, :]).then_inc(y_done, 1)
                elif part == "Z":
                    at(pe, xt_ready, u, 2, 1)
                    at(pe, y_ready, u, 2, 1)
                    product4(MI[0], lambda n: XT[:, n, :], lambda n: Y[:, n, :]).then_inc(z_done, 1)
                elif part == "XT2":
                    at(pe, y_ready, u, 2, 1)
                    at(pe, x_merged, u, 2, 2)
                    transpose4(MI[1], lambda n: X[:, n, :]).then_inc(xt_done, 1)
                elif part == "Y2":
                    at(pe, x_merged, u, 2, 2)
                    product4(MI[0], lambda n: ab[:, bh, n, 0, :], lambda n: X[:, n, :]).then_inc(y_done, 1)
                elif part == "ZT":
                    at(pe, xt_ready, u, 2, 2)
                    at(pe, y_ready, u, 2, 2)
                    product4(MI[1], lambda n: Y[:, n, :], lambda n: XT[:, n, :]).then_inc(z_done, 1)
                elif part == "TV":
                    at(pe, y_ready, u, 2, 2)
                    at(pe, xt_merged, u, 2, 2)
                    product4(MI[0], lambda n: XT[:, n, :], lambda n: vs[:, n, :]).then_inc(tv_done, 1)
                elif part == "TK":
                    at(pe, xt_merged, u, 2, 2)
                    product4(MI[1], lambda n: ks[:, n, :], lambda n: XT[:, n, :]).then_inc(tk_done, 1)

            def chunk_u(h, b, c):
                _, bh, u, live = unit(h, b, 0)
                if not live or c == 0:
                    return
                r = C * (c % 2)
                at(pe, s_ready, u, 7, c)
                if c == 1:
                    at(pe, tk_ready, u, 1, 1)
                pe.matmul(CH[r:r + C, 0:HD], tk[:, bh % 2, c // 2, r:r + C], St[:, c % 2, :],
                          start=True, stop=True).then_inc(ups_done, 1)

            def chunk_so(h, b, c):
                _, bh, u, live = unit(h, b, 0)
                if not live:
                    return
                r, n = C * (c % 2), c // 2
                at(pe, u_ready, u, 8, c + 1)
                if c < NCH - 1:
                    if c == 0:
                        at(pe, kh_ready, u, 1, 1)
                    pe.matmul(CH[:, HD:2 * HD], kh[:, bh % 2, n, :], U[:, c % 2, :],
                              start=True, stop=True).then_inc(sps_done, 1)
                if c == 0:
                    at(pe, og_ready, u - 1, 1, 1)
                o = OB[r:r + C, HD * n:HD * n + HD]
                if c:
                    pe.matmul(o, kq[:, bh, 1, C * c:C * c + C], St[:, c % 2, :], start=True, stop=False)
                pe.matmul(o, ab[:, bh, n, 1, r:r + C], U[:, c % 2, :], start=(c == 0), stop=True).then_inc(o_done, 1)

            def output(h, b, part):
                hh, bh, u, live = unit(h, b, -1)
                if not live:
                    return
                if part == "T":
                    at(pe, og_ready, u, 1, 1)
                    if not isinstance(u, int) or u + 1 < UNITS:
                        at(pe, tv_ready, u + 1, 1, 1)
                    transpose4(MI[0], lambda n: og[:, n, :]).then_inc(ogtr_done, 1)
                else:
                    at(pe, ogt_ready, u, 1, 1)
                    if part:
                        at(pe, acc_step, u, 4, 2)
                    else:
                        at(pe, wo_loaded, hh, 16, 16)
                    for n in range(2):
                        mm = pe.matmul(MI[0][:, D * n:D * n + D], ogT[:, 2 * part + n, :], wo[:, :], start=True, stop=True)
                    mm.then_inc(wo_done, 1)

            def slot(h, b):
                level(h, b, 0)
                chunk_so(h, b, 0)
                output(h, b, "T")
                project(h, b, 0)

                chunk_u(h, b, 1)
                inverse(h, b, "V")
                chunk_so(h, b, 1)
                level(h, b, 1)
                project(h, b, 1)

                chunk_u(h, b, 2)
                output(h, b, 0)
                chunk_so(h, b, 2)
                level(h, b, 2)
                inverse(h, b, "K")
                project(h, b, 2)

                chunk_u(h, b, 3)
                output(h, b, 1)
                chunk_so(h, b, 3)
                level(h, b, 3)
                inverse(h, b, "KH")
                project(h, b, 3)

                chunk_u(h, b, 4)
                inverse(h, b, "XT")
                inverse(h, b, "Y")
                chunk_so(h, b, 4)
                level(h, b, 4)
                project(h, b, 4)

                chunk_u(h, b, 5)
                inverse(h, b, "Z")
                chunk_so(h, b, 5)
                level(h, b, 5)
                sums(h, b)

                chunk_u(h, b, 6)
                inverse(h, b, "XT2")
                chunk_so(h, b, 6)
                inverse(h, b, "Y2")

                chunk_u(h, b, 7)
                inverse(h, b, "ZT")
                chunk_so(h, b, 7)
                inverse(h, b, "TV")
                inverse(h, b, "TK")

            run(pe, slot)

        @block.vector
        def _(dve):
            dve.wait_ge(const_loaded, 16 * 11)
            dve.wait_ge(const_ready, 8)

            def params(h, b):
                hh, bh, u, live = unit(h, b, 4)
                if not live:
                    return
                p = bh % 2
                at(dve, conv_step, u - 2, 9, 9)
                at(dve, dec_ready, u - 2, 1, 1)
                dve.tensor_tensor(par[:, p, :], par_all[:, :, :].rearrange("p h k -> p (h k)")[:, bass.ds(hh * NPAR, NPAR)],
                                   par_one[:, :], ALU.mult).then_inc(par_ready, 1)

            def gated(h, b):
                _, bh, u, live = unit(h, b, -1)
                if not live:
                    return
                at(dve, o_done, u, 8, 8)
                at(dve, ogtr_done, u - 1, 1, 1)
                at(dve, oss_ready, u - 1, 4, 4)
                dve.tensor_tensor(og[:, :, :], OB[:, :].rearrange("p (n d) -> p n d", n=TPB), gate[:, bh, :, :],
                                  ALU.mult).then_inc(og_ready, 1)

            def norms(h, b):
                hh, bh, u, live = unit(h, b, 2)
                if not live:
                    return
                at(dve, sums_done, u, 1, 1)
                at(dve, fin_step, u - 4, 4, 4)
                dve.tensor_scalar(rk[:, bh, 0, :], SUMS[:, 0:TPB], L2_EPS, None, ALU.add).then_inc(norm_step, 1)
                dve.tensor_scalar(rk[:, bh, 1, :], SUMS[:, TPB:2 * TPB], L2_EPS, float(HD),
                                  ALU.add, ALU.mult).then_inc(norm_step, 1)
                at(dve, norm_step, u, 5, 2)
                dve.reciprocal(r2[:, bh, :, :], rk[:, bh, :, :]).then_inc(norm_step, 1)
                at(dve, norm_step, u, 5, 3)
                bt = beta[:, :, :].rearrange("p h n -> p (h n)")[:, bass.ds(hh * NT + TPB * bh, TPB)]
                dve.tensor_tensor(bp[:, bh, 0, :], r2[:, bh, 0, :], bt, ALU.mult).then_inc(norm_step, 1)
                at(dve, norm_step, u, 5, 4)
                dve.tensor_scalar(bp[:, bh, 1, :], bp[:, bh, 0, :], -1.0, None, ALU.mult).then_inc(norm_step, 1)

            def final_scale(h, b):
                _, bh, u, live = unit(h, b, -1)
                if not live:
                    return
                at(dve, oss_ready, u, 4, 4)
                at(dve, fin_ready, u - 1, 2, 2)
                dve.scalar_tensor_tensor(out=fin[:, 0, :], in0=oss[:, :], scalar=1.0 / HD, in1=r2[:, bh, 1, :],
                                         op0=ALU.mult, op1=ALU.mult).then_inc(fin_step, 1)
                at(dve, fin_step, u, 4, 1)
                dve.tensor_scalar(fin[:, 1, :], fin[:, 0, :], RMS_EPS, None, ALU.add).then_inc(fin_step, 1)
                at(dve, fin_step, u, 4, 2)
                dve.reciprocal(fin[:, 2, :], fin[:, 1, :]).then_inc(fin_step, 1)
                at(dve, fin_step, u, 4, 3)
                dve.tensor_tensor(fin[:, 3, :], fin[:, 2, :], r2[:, bh, 1, :], ALU.mult).then_inc(fin_step, 1)

            def v_scale(h, b):
                hh, bh, u, live = unit(h, b, 2)
                if not live:
                    return
                bt = beta[:, :, :].rearrange("p h n -> p (h n)")[:, bass.ds(hh * NT + TPB * bh, TPB)]
                at(dve, rk_step, u, 2, 2)
                dve.tensor_tensor(bp[:, bh, 2, :], rk[:, bh, 1, :], bt, ALU.mult).then_inc(bv_ready, 1)

            def first_scale(h, b):
                _, bh, u, live = unit(h, b, 2)
                if not live:
                    return
                at(dve, qkv_ready, u, 3, 2)
                at(dve, dec_ready, u, 1, 1)
                at(dve, sq_ready, u, 2, 2)
                dve.tensor_tensor(kq[:, bh, 0, :], kr[:, bh, :], dec[:, bh, :], ALU.mult).then_inc(scale_step, 1)
                dve.tensor_tensor(kq[:, bh, 1, :], kq[:, bh, 2, :], dec[:, bh, :], ALU.mult).then_inc(scale_step, 1)

            def scale(h, b, k):
                _, bh, u, live = unit(h, b, 2)
                if not live:
                    return
                m = LEVELS[k]
                nb = S // (2 * m)
                at(dve, lev_done, u, 6, k + 1)
                at(dve, scale_step, u, SCALES, after_scale(k))
                if k == 0:
                    src = dec[:, bh, :]
                else:
                    off = S - 2 * (S // (2 * m)) * 2
                    src = tot[:, bh, off:off + 2 * nb]
                pair = src.rearrange("p (a t) -> p a t", t=2)
                lo, up = pair[:, :, 0], pair[:, :, 1]
                dst = S - 2 * nb
                kv = kr[:, bh, :].rearrange("p (a t m) -> p a t m", t=2, m=m)
                dve.tensor_tensor(kv[:, :, 0, :], kv[:, :, 0, :], bc(up, m), ALU.mult).then_inc(scale_step, 1)
                qv = kq[:, bh, 0:2, :].rearrange("p z (a t m) -> p z a t m", t=2, m=m)
                dve.tensor_tensor(qv[:, :, :, 1, :], qv[:, :, :, 1, :],
                                  lo.unsqueeze(1).unsqueeze(3).to_broadcast([128, 2, nb, m]), ALU.mult).then_inc(scale_step, 1)
                if 1 <= k < 5:
                    at(dve, lev_read, u, 10, k + 2)
                dve.tensor_tensor(tot[:, bh, dst:dst + nb], lo, up, ALU.mult).then_inc(scale_step, 1)
                if k in ROUNDED:
                    at(dve, scale_step, u, SCALES, after_scale(k) + 3)
                    for x in (kv[:, :, 0, :], qv[:, :, :, 1, :]):
                        dve.tensor_scalar(x, x, TINY, -TINY, ALU.add, ALU.add).then_inc(scale_step, 1)

            def pick(h, b, k):
                _, bh, u, live = unit(h, b, 2)
                if not live:
                    return
                if k == 0:
                    at(dve, lev_done, u, 6, 1)
                    s0 = SC[0][:, 0:TPB * 96].rearrange("p (n w) -> p n w", n=TPB)
                    at(dve, ab_out, u - 1, 32, 32)
                    at(dve, ab_ready, u - 1, 4, 4)
                    dve.tensor_tensor(comp[:, :, :], s0[:, :, 0:64], tiles_bc(first[:, :], TPB), ALU.mult).then_inc(lev_read, 1)
                    dve.tensor_tensor(own[:, :, :], s0[:, :, 64:96], tiles_bc(masks[:, 256:288], TPB), ALU.mult).then_inc(lev_read, 1)
                    at(dve, lev_read, u, 10, 2)
                    dve.tensor_tensor(comp[:, :, 32:64], comp[:, :, 32:64], own[:, :, :], ALU.add).then_inc(lev_read, 1)
                elif k < 5:
                    dve.copy_predicated(comp[:, :, :], tiles_bc(masks[:, 64 * k - 64:64 * k].bitcast(U32), TPB),
                                        SC[k % 2][:, 0:TPB * 64].rearrange("p (n w) -> p n w", n=TPB)).then_inc(lev_read, 1)
                    if k == 4:
                        at(dve, lev_read, u, 10, 7)
                        dve.tensor_scalar(comp[:, :, :], comp[:, :, :], TINY, -TINY, ALU.add, ALU.add).then_inc(lev_read, 1)
                else:
                    at(dve, lev_done, u, 6, 6)
                    at(dve, o_done, u - 4, 8, 8)
                    for g in (0, 64):
                        dve.tensor_scalar(ab[g:g + 32, bh, :, :, g + 32:g + 64],
                                          SC[1][g:g + 32, 0:TPB * 64].rearrange("p (n z w) -> p n z w", n=TPB, z=2),
                                          TINY, -TINY, ALU.add, ALU.add).then_inc(lev_read, 1)

            def conv(h, b, i):
                _, bh, u, live = unit(h, b, 3)
                if not live:
                    return
                at(dve, tap_ready, u, 3, i + 1)
                at(dve, proj_read, u, 5, i + 1)
                for j in range(TAPS - 1):
                    if j:
                        at(dve, conv_step, u, 9, 3 * i + j)
                    dve.scalar_tensor_tensor(out=y[i][:, :], in0=xp[i][:, j:j + S],
                                             scalar=par[:, bh % 2, TAPS * i + j:TAPS * i + j + 1], in1=y[i][:, :],
                                             op0=ALU.mult, op1=ALU.add).then_inc(conv_step, 1)

            def softplus_min(h, b):
                _, bh, u, live = unit(h, b, 3)
                if not live:
                    return
                at(dve, proj_read, u, 5, 4)
                at(dve, sp_ready, u - 1, 1, 1)
                dve.tensor_scalar(ge[:, :], gx[:, :], SP_MAX, None, ALU.min).then_inc(gmin_ready, 1)

            def softplus_max(h, b):
                _, bh, u, live = unit(h, b, 3)
                if not live:
                    return
                at(dve, g_step, u, 2, 2)
                at(dve, dec_ready, u - 1, 1, 1)
                dve.tensor_tensor(gx[:, :], gx[:, :], ge[:, :], ALU.max).then_inc(sp_ready, 1)

            def inverse(h, b, part):
                _, bh, u, live = unit(h, b, 1)
                if not live:
                    return
                mi = [m[:, :].rearrange("p (n j) -> p n j", n=TPB) for m in MI]
                if part in ("Y", "Y2"):
                    at(dve, y_done, u, 2, 1 + (part == "Y2"))
                    at(dve, z_done, u if part == "Y2" else u - 1, 2, 1 + (part == "Y"))
                    dve.tensor_tensor(Y[:, :, :], mi[part == "Y"], bc(bp[:, bh, 1, :], 128), ALU.mult).then_inc(y_ready, 1)
                elif part == "Z":
                    at(dve, z_done, u, 2, 1)
                    dve.tensor_tensor(zm[:, :, :], mi[0], tiles_bc(up16[:, :], TPB), ALU.mult).then_inc(x_merged, 1)
                    at(dve, x_merged, u, 2, 1)
                    dve.tensor_tensor(X[:, :, :], X[:, :, :], zm[:, :, :], ALU.add).then_inc(x_merged, 1)
                elif part == "ZT":
                    at(dve, z_done, u, 2, 2)
                    for g in (0, 64):
                        dve.tensor_copy(XT[g:g + 32, :, g + 32:g + 64], mi[1][g:g + 32, :, g + 32:g + 64]).then_inc(xt_merged, 1)

            def chunk_u(h, b, c):
                _, bh, u, live = unit(h, b, 0)
                if not live:
                    return
                r, n = C * (c % 2), c // 2
                dst, src = U[r:r + C, c % 2, :], tv[r:r + C, bh % 2, n, :]
                if c == 0:
                    at(dve, tv_ready, u, 1, 1)
                    at(dve, o_done, u - 1, 8, 8)
                    dve.tensor_copy(dst, src).then_inc(u_ready, 1)
                else:
                    at(dve, ups_done, u, 7, c)
                    if c >= 2:
                        at(dve, o_done, u, 8, c - 1)
                    dve.tensor_tensor(dst, CH[r:r + C, 0:HD], src, ALU.add).then_inc(u_ready, 1)

            def chunk_s(h, b, c):
                _, bh, u, live = unit(h, b, 0)
                if not live or c == NCH - 1:
                    return
                at(dve, sps_done, u, 7, c + 1)
                nxt = St[:, (c + 1) % 2, :]
                if c == 0:
                    dve.tensor_copy(nxt, CH[:, HD:2 * HD]).then_inc(s_ready, 1)
                else:
                    at(dve, o_done, u, 8, c)
                    at(dve, s_ready, u, 7, c)
                    dve.scalar_tensor_tensor(out=nxt, in0=St[:, c % 2, :], scalar=tot[:, bh, S - 16 + c:S - 15 + c],
                                             in1=CH[:, HD:2 * HD], op0=ALU.mult, op1=ALU.add).then_inc(s_ready, 1)

            def add_output(h, b, half):
                _, bh, u, live = unit(h, b, -1)
                if not live:
                    return
                at(dve, fin_ready, u, 2, 2)
                at(dve, acc_step, u - 4, 4, 4)
                at(dve, wo_done, u, 2, half + 1)
                for n in (2 * half, 2 * half + 1):
                    a = acc[:, TPB * bh + n, :]
                    dve.scalar_tensor_tensor(out=a, in0=MI[0][:, D * (n % 2):D * (n % 2) + D],
                                             scalar=fin[:, 4, n:n + 1], in1=a, op0=ALU.mult, op1=ALU.add).then_inc(acc_step, 1)

            def slot(h, b):
                first_scale(h, b)
                chunk_u(h, b, 0)
                gated(h, b)
                params(h, b)
                chunk_s(h, b, 0)

                chunk_u(h, b, 1)
                scale(h, b, 0)
                pick(h, b, 0)
                chunk_s(h, b, 1)
                final_scale(h, b)
                conv(h, b, 0)

                chunk_u(h, b, 2)
                scale(h, b, 1)
                pick(h, b, 1)
                chunk_s(h, b, 2)
                add_output(h, b, 0)
                conv(h, b, 1)

                chunk_u(h, b, 3)
                scale(h, b, 2)
                pick(h, b, 2)
                chunk_s(h, b, 3)
                add_output(h, b, 1)
                conv(h, b, 2)

                chunk_u(h, b, 4)
                scale(h, b, 3)
                pick(h, b, 3)
                inverse(h, b, "Y")
                chunk_s(h, b, 4)
                softplus_min(h, b)

                chunk_u(h, b, 5)
                scale(h, b, 4)
                pick(h, b, 4)
                chunk_s(h, b, 5)
                inverse(h, b, "Z")
                norms(h, b)

                chunk_u(h, b, 6)
                scale(h, b, 5)
                chunk_s(h, b, 6)
                softplus_max(h, b)
                inverse(h, b, "Y2")
                pick(h, b, 5)

                chunk_u(h, b, 7)
                inverse(h, b, "ZT")
                v_scale(h, b)

            run(dve, slot)

        @block.scalar
        def _(act):
            act.wait_ge(const_loaded, 16 * 11)
            act.activation(alog[:, :], alog[:, :], ACT.Exp).then_inc(nega_exp, 1)
            act.wait_ge(nega_exp, 1)
            act.mul(par_all[:, :, 13], alog[:, :], -1.0).then_inc(const_ready, 1)

            def evacuate(h, b, i):
                _, bh, u, live = unit(h, b, 3)
                if not live:
                    return
                bank = PJ[(bh + i) % 2]
                at(act, proj_done, u, 5, i + 1)
                if i == 3:
                    at(act, dec_ready, u - 1, 1, 1)
                    act.activation(gx[:, :], bank[:, :], ACT.Identity, bias=par[:, bh % 2, 12:13]).then_inc(proj_read, 1)
                elif i < 3:
                    at(act, par_ready, u, 1, 1)
                    at(act, qkv_ready, u - 1, 3, i + 1)
                    own = par[:, bh % 2, TAPS * i + TAPS - 1:TAPS * i + TAPS]
                    act.activation(y[i][:, :], bank[:, :], ACT.Copy, scale=own).then_inc(tap_ready, 1)
                    at(act, conv_step, u - 1, 9, 3 * i + 3)
                    act.activation(xp[i][:, TAPS - 1:], bank[:, :], ACT.Copy).then_inc(proj_read, 1)
                else:
                    at(act, og_ready, u - 4, 1, 1)
                    act.activation(gate[:, bh, :, :], bank[:, :].rearrange("p (n d) -> p n d", n=TPB),
                                   ACT.Sigmoid).then_inc(proj_read, 1)

            def decay(h, b, part):
                _, bh, u, live = unit(h, b, 3)
                if not live:
                    return
                if part == 0:
                    at(act, gmin_ready, u, 1, 1)
                    act.activation(ge[:, :], ge[:, :], ACT.Exp).then_inc(g_step, 1)
                    at(act, g_step, u, 2, 1)
                    act.activation(ge[:, :], ge[:, :], ACT.Ln, bias=1.0).then_inc(g_step, 1)
                else:
                    at(act, sp_ready, u, 1, 1)
                    at(act, scale_step, u - 4, SCALES, SCALES)
                    act.activation(dec[:, bh, :], gx[:, :], ACT.Exp, scale=par[:, bh % 2, 13:14]).then_inc(dec_ready, 1)

            def sigmoid(h, b, i):
                _, bh, u, live = unit(h, b, 3)
                if not live:
                    return
                at(act, conv_step, u, 9, 3 * i + 3)
                at(act, qkv_ready, u - 1, 3, i + 1)
                act.activation(sg[i][:, :], y[i][:, :], ACT.Sigmoid).then_inc(sig_ready, 1)

            def square(h, b):
                _, bh, u, live = unit(h, b, 3)
                if not live:
                    return
                at(act, sums_done, u - 1, 1, 1)
                for i in range(2):
                    at(act, qkv_ready, u, 3, i + 1)
                    act.activation(sq[:, i, :], (kr[:, bh, :], kq[:, bh, 2, :])[i], ACT.Square).then_inc(sq_ready, 1)

            def output_squares(h, b):
                _, bh, u, live = unit(h, b, -1)
                if not live:
                    return
                at(act, og_ready, u, 1, 1)
                at(act, fin_step, u - 1, 4, 1)
                for n in range(TPB):
                    if not (isinstance(u, int) and u == 0 and n == 0):
                        at(act, oss_ready, u, 4, n) if n else at(act, oss_ready, u - 1, 4, 4)
                    act.activation(ogs[:, :], og[:, n, :], ACT.Square, accum_out=oss[:, n:n + 1]).then_inc(oss_ready, 1)

            def k_root(h, b):
                _, bh, u, live = unit(h, b, 2)
                if not live:
                    return
                at(act, norm_step, u, 5, 3)
                act.activation(rk[:, bh, 0, :], r2[:, bh, 0, :], ACT.Ln).then_inc(rk_step, 1)
                at(act, rk_step, u, 2, 1)
                act.activation(rk[:, bh, 1, :], rk[:, bh, 0, :], ACT.Exp, scale=0.5).then_inc(rk_step, 1)

            def final_root(h, b):
                _, bh, u, live = unit(h, b, -1)
                if not live:
                    return
                at(act, fin_step, u, 4, 4)
                at(act, acc_step, u - 1, 4, 4)
                act.activation(fin[:, 0, :], fin[:, 3, :], ACT.Ln).then_inc(fin_ready, 1)
                at(act, fin_ready, u, 2, 1)
                act.activation(fin[:, 4, :], fin[:, 0, :], ACT.Exp, scale=0.5).then_inc(fin_ready, 1)

            def spread(h, b):
                _, bh, u, live = unit(h, b, 2)
                if not live:
                    return
                at(act, lev_read, u, 10, 8)
                at(act, o_done, u - 4, 8, 8)
                for g in range(0, 128, 32):
                    act.activation(ab[g:g + 32, bh, :, :, g:g + 32],
                                   comp[g:g + 32, :, :].rearrange("p n (z w) -> p n z w", z=2), ACT.Copy).then_inc(ab_ready, 1)

            def inverse(h, b, part):
                _, bh, u, live = unit(h, b, 1)
                if not live:
                    return
                mi = [m[:, :].rearrange("p (n j) -> p n j", n=TPB) for m in MI]
                if part == "V":
                    at(act, vtr_done, u, 1, 1)
                    at(act, tv_done, u - 1, 1, 1)
                    at(act, bv_ready, u, 1, 1)
                    for n in range(TPB):
                        act.activation(vs[:, n, :], mi[1][:, n, :], ACT.Copy, scale=bp[:, bh, 2, n:n + 1]).then_inc(vs_ready, 1)
                elif part == "K":
                    at(act, ktr_done, u, 1, 1)
                    at(act, tk_done, u - 1, 1, 1)
                    at(act, norm_step, u, 5, 5)
                    for n in range(TPB):
                        act.activation(ks[:, n, :], mi[1][:, n, :], ACT.Copy, scale=bp[:, bh, 1, n:n + 1]).then_inc(ks_ready, 1)
                elif part == "XT":
                    at(act, xt_done, u, 2, 1)
                    at(act, tk_done, u - 1, 1, 1)
                    act.activation(XT[:, :, :], mi[0], ACT.Copy).then_inc(xt_ready, 1)
                elif part == "XT2":
                    at(act, xt_done, u, 2, 2)
                    at(act, xt_ready, u, 2, 1)
                    act.activation(XT[:, :, :], mi[1], ACT.Copy).then_inc(xt_ready, 1)
                elif part == "KH":
                    at(act, khtr_done, u, 1, 1)
                    at(act, sps_done, u - 2, 7, 7)
                    act.activation(kh[:, bh % 2, :, :], mi[1], ACT.Copy).then_inc(kh_ready, 1)
                elif part == "TV":
                    at(act, tv_done, u, 1, 1)
                    at(act, u_ready, u - 2, 8, 8)
                    act.activation(tv[:, bh % 2, :, :], mi[0], ACT.Copy).then_inc(tv_ready, 1)
                elif part == "TK":
                    at(act, tk_done, u, 1, 1)
                    at(act, ups_done, u - 2, 7, 7)
                    act.activation(tk[:, bh % 2, :, :], mi[1], ACT.Copy).then_inc(tk_ready, 1)

            def output_T(h, b):
                _, bh, u, live = unit(h, b, -1)
                if not live:
                    return
                at(act, ogtr_done, u, 1, 1)
                at(act, wo_done, u - 1, 2, 2)
                act.activation(ogT[:, :, :], MI[0][:, :].rearrange("p (n j) -> p n j", n=TPB), ACT.Copy,
                               scale=onorm[:, :]).then_inc(ogt_ready, 1)

            def slot(h, b):
                evacuate(h, b, 0)
                output_T(h, b)
                output_squares(h, b)
                evacuate(h, b, 1)
                final_root(h, b)
                inverse(h, b, "V")
                act.preload_act_table_set("sigmoid_and_others")
                evacuate(h, b, 2)
                sigmoid(h, b, 0)
                inverse(h, b, "K")
                sigmoid(h, b, 1)
                inverse(h, b, "KH")
                evacuate(h, b, 3)
                inverse(h, b, "XT")
                sigmoid(h, b, 2)
                evacuate(h, b, 4)
                act.preload_act_table_set("natural_log_exp_and_others")
                decay(h, b, 0)
                k_root(h, b)
                spread(h, b)
                inverse(h, b, "XT2")
                decay(h, b, 1)
                square(h, b)
                inverse(h, b, "TV")
                inverse(h, b, "TK")

            run(act, slot)


def norm_transpose(nc, ident, acc, banks, zT, w_dram, x_dram, layer):
    with ExitStack() as ctx:
        def sb(name, shape, dt=F32):
            return ctx.enter_context(nc.sbuf_tensor(f"{name}{int(layer)}", shape, dt))

        def sem(name):
            return ctx.enter_context(nc.semaphore(f"{name}{int(layer)}"))

        stats = sb("nstats", [128, NT, 6])
        mv = sb("nmv", [128, NT, 2])
        r = sb("nr", [128, 4, NT])
        rows = sb("nrows", [128, 4, D])
        w = sb("nw", [128, DC])
        x = sb("nx", [128, NT, D])
        loaded, added, stat_step, agg_step, r_step = (sem(n) for n in ("nloaded", "nadded", "nstat", "nagg", "nrstep"))
        root_ready, rows_ready, tr_done, z_ready = (sem(n) for n in ("nroot", "nrows_ready", "ntr", "nz"))
        block = ctx.enter_context(nc.Block())

        @block.sync
        def _(sp):
            if layer:
                xv = x_dram.rearrange("b (n p) d -> p (b n) d", p=128)
                for i in range(4):
                    sp.dma_start(x[:, 4 * i:4 * i + 4, :], xv[:, 4 * i:4 * i + 4, :]).then_inc(loaded, 16)
                    sp.wait_ge(loaded, 16 * i + 16)
            else:
                sp.dma_start(w[:, :], w_dram.rearrange("(c p) -> p c", p=128), allow_slow_non_contiguous=True).then_inc(loaded, 16)

        @block.vector
        def _(dve):
            for i in range(NT):
                if layer:
                    dve.wait_ge(loaded, 16 * (i // 4 + 1))
                    dve.tensor_tensor(acc[:, i, :], acc[:, i, :], x[:, i, :], ALU.add).then_inc(added, 1)
                    dve.wait_ge(added, i + 1)
                dve.bn_stats(stats[:, i, :], acc[:, i, :]).then_inc(stat_step, 1)
            for i in range(NT):
                dve.wait_ge(stat_step, i + 1)
                dve.bn_aggr(mv[:, i, :], stats[:, i, :]).then_inc(agg_step, 1)
            dve.wait_ge(agg_step, NT)
            if layer:
                dve.tensor_scalar(r[:, 0, :], mv[:, :, 1], LN_EPS, None, ALU.add).then_inc(r_step, 1)
            else:
                dve.tensor_tensor(r[:, 3, :], mv[:, :, 0], mv[:, :, 0], ALU.mult).then_inc(r_step, 1)
                dve.wait_ge(r_step, 1)
                dve.scalar_tensor_tensor(out=r[:, 0, :], in0=r[:, 3, :], scalar=RMS_EPS, in1=mv[:, :, 1],
                                         op0=ALU.add, op1=ALU.add).then_inc(r_step, 1)
            dve.wait_ge(root_ready, 1)
            dve.reciprocal(r[:, 2, :], r[:, 1, :]).then_inc(r_step, 1)
            dve.wait_ge(r_step, 2 if layer else 3)
            for i in range(NT):
                if i >= 4:
                    dve.wait_ge(tr_done, 2 * (i // 4))
                if layer:
                    dve.tensor_scalar(rows[:, i % 4, :], acc[:, i, :], mv[:, i, 0:1], r[:, 2, i:i + 1],
                                      ALU.subtract, ALU.mult).then_inc(rows_ready, 1)
                else:
                    dve.tensor_scalar(rows[:, i % 4, :], acc[:, i, :], r[:, 2, i:i + 1], None, ALU.mult).then_inc(rows_ready, 1)

        @block.scalar
        def _(act):
            act.wait_ge(r_step, 1 if layer else 2)
            act.activation(r[:, 1, :], r[:, 0, :], ACT.Sqrt).then_inc(root_ready, 1)
            if not layer:
                act.wait_ge(loaded, 16)
            for i in range(4):
                for c in range(DC):
                    act.wait_ge(tr_done, 2 * i + c + 1)
                    act.activation(zT[:, c, 512 * i:512 * i + 512], banks[c][:, :], ACT.Copy,
                                   scale=1.0 if layer else w[:, c:c + 1]).then_inc(z_ready, 1)
            act.wait_ge(z_ready, 8)

        @block.tensor
        def _(pe):
            for i in range(4):
                pe.wait_ge(rows_ready, 4 * i + 4)
                for c in range(DC):
                    if i:
                        pe.wait_ge(z_ready, 2 * (i - 1) + c + 1)
                    for n in range(4):
                        mm = pe.transpose(banks[c][:, 128 * n:128 * n + 128], rows[:, n, 128 * c:128 * c + 128], ident[:, :])
                    mm.then_inc(tr_done, 1)


def route(nc, banks, zT, gate_dram, comb):
    with ExitStack() as ctx:
        def sb(name, shape, dt=F32):
            return ctx.enter_context(nc.sbuf_tensor(name, shape, dt))

        def sem(name):
            return ctx.enter_context(nc.semaphore(name))

        gw = sb("gw", [128, DC, E])
        mx = sb("mx", [128, NT, 2])
        lg = sb("lg", [128, NT, E])
        pb = sb("pb", [128, NT, E])
        top = sb("top", [128, NT, E])
        rest = sb("rest", [128, NT, E])
        gw_loaded, logits_done, step, exp_ready = sem("gw_loaded"), sem("logits_done"), sem("route_step"), sem("exp_ready")
        block = ctx.enter_context(nc.Block())
        lo = banks[0][:, 0:NT * E].rearrange("p (n e) -> p n e", e=E)

        @block.sync
        def _(sp):
            sp.dma_start(gw[:, :, :], gate_dram.rearrange("(c p) e -> p c e", p=128)).then_inc(gw_loaded, 16)

        @block.tensor
        def _(pe):
            pe.wait_ge(gw_loaded, 16)
            for n in range(NT):
                for c in range(DC):
                    mm = pe.matmul(lo[:, n, :], zT[:, c, 128 * n:128 * n + 128], gw[:, c, :], start=(c == 0), stop=(c == DC - 1))
            mm.then_inc(logits_done, 1)

        @block.scalar
        def _(act):
            act.wait_ge(step, 2)
            act.activation(pb[:, :, :], lg[:, :, :], ACT.Exp).then_inc(exp_ready, 1)

        @block.vector
        def _(dve):
            dve.wait_ge(logits_done, 1)
            dve.tensor_reduce(mx[:, :, 0], lo, AX.X, ALU.max).then_inc(step, 1)
            dve.wait_ge(step, 1)
            dve.tensor_tensor(lg[:, :, :], lo, bc(mx[:, :, 0], E), ALU.subtract).then_inc(step, 1)
            dve.wait_ge(exp_ready, 1)
            dve.tensor_reduce(mx[:, :, 0], pb[:, :, :], AX.X, ALU.add).then_inc(step, 1)
            dve.wait_ge(step, 3)
            dve.reciprocal(mx[:, :, 1], mx[:, :, 0]).then_inc(step, 1)
            dve.wait_ge(step, 4)
            dve.tensor_tensor(lg[:, :, :], pb[:, :, :], bc(mx[:, :, 1], E), ALU.mult).then_inc(step, 1)
            dve.wait_ge(step, 5)
            for n in range(NT):
                dve.max(top[:, n, :], lg[:, n, :]).then_inc(step, 1)
            dve.wait_ge(step, 5 + NT)
            dve.memset(top[:, :, 2:E], -1.0).then_inc(step, 1)
            dve.wait_ge(step, 6 + NT)
            for n in range(NT):
                dve.match_replace(rest[:, n, :], top[:, n, :], lg[:, n, :], 0.0).then_inc(step, 1)
            dve.wait_ge(step, 6 + 2 * NT)
            dve.tensor_tensor(lg[:, :, :], lg[:, :, :], rest[:, :, :], ALU.subtract).then_inc(step, 1)
            dve.wait_ge(step, 7 + 2 * NT)
            dve.tensor_reduce(mx[:, :, 0], lg[:, :, :], AX.X, ALU.add).then_inc(step, 1)
            dve.wait_ge(step, 8 + 2 * NT)
            dve.reciprocal(mx[:, :, 1], mx[:, :, 0]).then_inc(step, 1)
            dve.wait_ge(step, 9 + 2 * NT)
            dve.tensor_tensor(comb[:, 1:, :].rearrange("p e n -> p n e"), lg[:, :, :], bc(mx[:, :, 1], E), ALU.mult).then_inc(step, 1)
            dve.memset(comb[:, 0, :], 1.0).then_inc(step, 1)
            dve.wait_ge(step, 11 + 2 * NT)


def gated_mlps(nc, name, acc, banks, zT, load_up, load_down, first, pairs, comb):
    NB = TOK // 512
    NI = I // 128
    with ExitStack() as ctx:
        def sb(n, shape, dt=F32):
            return ctx.enter_context(nc.sbuf_tensor(name + n, shape, dt))

        def sem(n):
            return ctx.enter_context(nc.semaphore(name + n))

        up = sb("up", [128, 2, DC, 2 * I])
        down = sb("down", [128, 2, NI, D])
        act_g = sb("act_g", [128, 2, 512])
        mid = sb("mid", [128, 2, NI, 512])
        up_loaded, down_loaded = [sem("up_loaded0"), sem("up_loaded1")], [sem("down_loaded0"), sem("down_loaded1")]
        gate_done, up_done, silu_ready, mid_ready = (sem(n) for n in ("gate_done", "up_done", "silu", "mid_r"))
        down_done, acc_step = sem("down_done"), sem("acc_step")
        passes = first + 2 * pairs
        PG, PU, PD = banks[0:2], banks[2:4], banks[4:6]

        def run(eng, one):
            for g in range(first):
                one(g, g % 2, g // 2)
            if pairs:
                with eng.Fori(0, pairs) as i:
                    for j in range(2):
                        one(first + 2 * i + j, (first + j) % 2, i + (first + j) // 2)

        block = ctx.enter_context(nc.Block())

        @block.sync
        def _(sp):
            def one(g, q):
                if not isinstance(g, int) or g >= 2:
                    at(sp, up_done, (g - 2) * NB + NB - 1, 4, 4)
                for dst, src in load_up(up, q, g):
                    sp.dma_start(dst, src).then_inc(up_loaded[q], 16)
                if not isinstance(g, int) or g >= 2:
                    at(sp, down_done, (g - 2) * NB + NB - 1, 2, 2)
                sp.dma_start(down[:, q, :, :], load_down(g)).then_inc(down_loaded[q], 16)

            for g in range(first):
                one(g, g % 2)
            if pairs:
                for g in range(first, 3):
                    one(g, g % 2)
                with sp.Fori(0, pairs - 1) as i:
                    for j in range(2):
                        one(3 + 2 * i + j, (3 + j) % 2)

        @block.tensor
        def _(pe):
            def first_product(g, q, r, k):
                s = g * NB + k
                if k == 0:
                    at(pe, up_loaded[q], r, 16 * UPD, 16 * UPD)
                for m in range(NI):
                    for which, (bank, free, done) in enumerate(((PG, silu_ready, gate_done), (PU, mid_ready, up_done))):
                        if m >= 2:
                            at(pe, free, s, 4, m - 1)
                        elif not (isinstance(s, int) and s == 0):
                            at(pe, free, s - 1, 4, m + 3)
                        for c in range(DC):
                            lo = I * which + 128 * m
                            mm = pe.matmul(bank[m % 2][:, :], up[:, q, c, lo:lo + 128], zT[:, c, 512 * k:512 * k + 512],
                                           start=(c == 0), stop=(c == DC - 1))
                        mm.then_inc(done, 1)

            def second_product(g, q, r, k):
                s = g * NB + k
                if k == 0:
                    at(pe, down_loaded[q], r, 16, 16)
                at(pe, mid_ready, s, 4, 4)
                for n in range(4):
                    if n % 2 == 0 and not (isinstance(s, int) and s == 0):
                        at(pe, acc_step, s - 1, 4, n + 2)
                    for m in range(NI):
                        mm = pe.matmul(PD[n // 2][:, D * (n % 2):D * (n % 2) + D], mid[:, k % 2, m, 128 * n:128 * n + 128],
                                       down[:, q, m, :], start=(m == 0), stop=(m == NI - 1))
                    if n % 2:
                        mm.then_inc(down_done, 1)

            def one(g, q, r):
                for k in range(NB):
                    first_product(g, q, r, k)
                    if k:
                        second_product(g, q, r, k - 1)
                    elif not (isinstance(g, int) and g == 0):
                        second_product(g - 1, 1 - q, r - 1 + q, NB - 1)

            run(pe, one)
            second_product(passes - 1, (passes - 1) % 2, (passes - 1) // 2, NB - 1)

        @block.scalar
        def _(act):
            def one(g, q, r):
                for k in range(NB):
                    s = g * NB + k
                    for m in range(NI):
                        at(act, gate_done, s, 4, m + 1)
                        if m >= 2:
                            at(act, mid_ready, s, 4, m - 1)
                        elif not (isinstance(s, int) and s == 0):
                            at(act, mid_ready, s - 1, 4, m + 3)
                        act.activation(act_g[:, m % 2, :], PG[m % 2][:, :], ACT.Silu).then_inc(silu_ready, 1)

            run(act, one)

        @block.vector
        def _(dve):
            def multiply(g, k):
                s = g * NB + k
                for m in range(NI):
                    at(dve, silu_ready, s, 4, m + 1)
                    at(dve, up_done, s, 4, m + 1)
                    if m == 0:
                        if k >= 2:
                            at(dve, down_done, s - 2, 2, 2)
                        elif not (isinstance(s, int) and s < 2):
                            at(dve, down_done, s - 2, 2, 2)
                    dve.tensor_tensor(mid[:, k % 2, m, :], act_g[:, m % 2, :], PU[m % 2][:, :], ALU.mult).then_inc(mid_ready, 1)

            def add(g, k):
                s = g * NB + k
                for n in range(4):
                    i = 4 * k + n
                    at(dve, down_done, s, 2, n // 2 + 1)
                    if n == 0:
                        at(dve, acc_step, s - 1, 4, 4)
                    src = PD[n // 2][:, D * (n % 2):D * (n % 2) + D]
                    if comb is None:
                        dve.tensor_tensor(acc[:, i, :], src, acc[:, i, :], ALU.add).then_inc(acc_step, 1)
                    else:
                        c = comb[:, :, :].rearrange("p e n -> p (e n)")[:, bass.ds(g * NT + i, 1)]
                        dve.scalar_tensor_tensor(out=acc[:, i, :], in0=src, scalar=c, in1=acc[:, i, :],
                                                 op0=ALU.mult, op1=ALU.add).then_inc(acc_step, 1)

            def one(g, q, r):
                for k in range(NB):
                    multiply(g, k)
                    if k:
                        add(g, k - 1)
                    elif not (isinstance(g, int) and g == 0):
                        add(g - 1, NB - 1)

            run(dve, one)
            add(passes - 1, NB - 1)
            dve.wait_ge(acc_step, 4 * NB * passes)


UPD = 2


def feed_forward(nc, t, ident, acc, banks, out):
    with ExitStack() as ctx:
        zT = ctx.enter_context(nc.sbuf_tensor("zT", [128, DC, TOK], F32))
        comb = ctx.enter_context(nc.sbuf_tensor("comb", [128, 1 + E, NT], F32))
        norm_transpose(nc, ident, acc, banks, zT, t["L0_attn_norm2_w"], None, False)

        w1 = t["L0_attn_w1"].rearrange("(c p) (g f) -> g p c f", p=128, f=I)
        w3 = t["L0_attn_w3"].rearrange("(c p) (g f) -> g p c f", p=128, f=I)
        w2 = t["L0_attn_w2"].rearrange("(g m p) n -> g p m n", p=128, m=I // 128)
        gated_mlps(nc, "f_", acc, banks, zT, lambda up, q, g: [(up[:, q, :, 0:I], w1[g]), (up[:, q, :, I:], w3[g])],
                   lambda g: w2[g], F // I, 0, None)

        norm_transpose(nc, ident, acc, banks, zT, None, t["L0_attn_x"], True)
        route(nc, banks, zT, t["L0_ffn_gate_w"], comb)

        bu = t["L0_ffn_base_gate_up"].rearrange("(c p) f -> p c f", p=128)
        bd = t["L0_ffn_base_down"].rearrange("(m p) n -> p m n", p=128)
        eu = t["L0_ffn_expert_gate_up"].rearrange("e (c p) f -> e p c f", p=128)
        ed = t["L0_ffn_expert_down"].rearrange("e (m p) n -> e p m n", p=128)

        def expert_up(up, q, g):
            src = bu if isinstance(g, int) and g == 0 else eu[g - 1]
            return [(up[:, q, :, 0:I], src[:, :, 0:I]), (up[:, q, :, I:], src[:, :, I:])]

        def expert_down(g):
            return bd if isinstance(g, int) and g == 0 else ed[g - 1]

        gated_mlps(nc, "e_", acc, banks, zT, expert_up, expert_down, 1, E // 2, comb)

        stored = ctx.enter_context(nc.semaphore("stored"))
        block = ctx.enter_context(nc.Block())
        ov = out.rearrange("b (n p) d -> p (b n) d", p=128)

        @block.sync
        def _(sp):
            for i in range(4):
                sp.dma_start(ov[:, 4 * i:4 * i + 4, :], acc[:, 4 * i:4 * i + 4, :]).then_inc(stored, 16)
            sp.wait_ge(stored, 64)


_INS = ["L0_attn_x", "L0_attn_norm1_w", "L0_attn_wq", "L0_attn_wk", "L0_attn_wv", "L0_attn_conv_q",
        "L0_attn_conv_k", "L0_attn_conv_v", "L0_attn_f_a", "L0_attn_f_b", "L0_attn_A_log", "L0_attn_dt_bias",
        "L0_attn_b_w", "L0_attn_g_a", "L0_attn_g_b", "L0_attn_onorm_w", "L0_attn_wo", "L0_attn_norm2_w",
        "L0_attn_w1", "L0_attn_w2", "L0_attn_w3", "L0_ffn_gate_w", "L0_ffn_base_gate_up", "L0_ffn_base_down",
        "L0_ffn_expert_gate_up", "L0_ffn_expert_down"]


def kernel(**inputs):
    import concourse.bacc as _bacc
    from concourse.bass_utils import run_bass_kernel_spmd as _run

    nc = _bacc.Bacc("TRN2", target_bir_lowering=False, num_devices=1)
    arrays, t = {}, {}
    for name, a in [*((n, np.ascontiguousarray(inputs[n])) for n in _INS), *shape_constants().items()]:
        arrays[f"in_{name}"] = a
        t[name] = nc.dram_tensor(f"in_{name}", a.shape, mybir.dt.from_np(a.dtype), kind="ExternalInput").ap()
    out = nc.dram_tensor("out_0", (B, S, D), F32, kind="ExternalOutput").ap()
    build(nc, t, out)
    r = _run(nc, [arrays], core_ids=[0])
    return r.results[0]["out_0"]
```
